# Optimizing a Trainium2 kernel written in Bass

```python
import numpy as np
import jax
import jax.numpy as jnp

def _softmax(x, axis=-1):
    return jax.nn.softmax(x, axis=axis)
def _gelu(x):
    return jax.nn.gelu(x, approximate=True)
def _silu(x):
    return jax.nn.silu(x)
def _sigmoid(x):
    return jax.nn.sigmoid(x)
def _layernorm(x, axis=-1, eps=1e-5):
    m = jnp.mean(x, axis=axis, keepdims=True)
    v = jnp.var(x, axis=axis, keepdims=True)
    return (x - m) / jnp.sqrt(v + eps)
def _scatter_add(tgt, idx, src, axis=0):
    return tgt.at[idx].add(src)
def _segment_sum(src, seg, n):
    return jax.ops.segment_sum(src, seg, n)

kernel_name = 'mk_metaformer_d2_conv_nchw128_8f74b1'

def setup_inputs(seed: int = 0):
    np.random.seed(seed)
    _w = jnp.asarray
    def _rec_inputs():
        import jax
        import jax.numpy as jnp
        _gk = jax.random.key(seed)
        x = -0.0009896 + 1 * jax.random.normal(jax.random.fold_in(_gk, 1), (16, 128, 28, 28), jnp.float32)
        return x
    x = _rec_inputs()
    def _L0_conv_setup():
        import jax, jax.numpy as jnp
        import numpy as np
        B, C, H, W_SP = (16, 128, 28, 28)
        F, KS, STRIDE, PAD = (128, 3, 1, 1)
        CHUNK = 4
        EPS = 1e-12

        def _patches(x):
            p = jax.lax.conv_general_dilated_patches(x, (KS, KS), (STRIDE, STRIDE), [(PAD, PAD), (PAD, PAD)], dimension_numbers=('NCHW', 'OIHW', 'NCHW'))
            b, k, ho, wo = p.shape
            return (p.reshape(b, k, ho * wo), ho, wo)
        key = jax.random.key(seed)
        kx, kw = jax.random.split(key)
        x = jax.random.normal(kx, (B, C, H, W_SP), dtype=jnp.float32)
        std = float(np.sqrt(2.0 / (C * KS * KS)))
        W = jax.random.normal(kw, (F, C, KS, KS), dtype=jnp.float32) * std
        return {'x': x, 'W': W}
    _L0_conv_all = _L0_conv_setup()
    _L0_conv_in = {k: v for k, v in _L0_conv_all.items() if k in ('W', )}
    del _L0_conv_all

    def _L0_ffn_setup():
        import jax, jax.numpy as jnp
        import numpy as np
        PADDED_SL = 8192
        TEMPERATURE = 1.0
        SIGMA_POW = 0.25

        def _stu_conv(phi, u, n):
            b, sl, d = u.shape
            sgn = jnp.where(jnp.arange(sl) % 2 == 0, 1.0, -1.0).astype(u.dtype)
            sgn3 = sgn[None, :, None]
            Vf = jnp.fft.rfft(phi, n=n, axis=0)
            Uf_p = jnp.fft.rfft(u, n=n, axis=1)
            Uf_m = jnp.fft.rfft(u * sgn3, n=n, axis=1)
            U_plus = jnp.fft.irfft(Vf[None, :, :, None] * Uf_p[:, :, None, :], n=n, axis=1)[:, :sl]
            U_minus = jnp.fft.irfft(Vf[None, :, :, None] * Uf_m[:, :, None, :], n=n, axis=1)[:, :sl]
            U_minus = U_minus * sgn[None, :, None, None]
            return (U_plus, U_minus)

        def _compute_spectral(u, sigma, phi, Mpp, Mpm):
            U_plus, U_minus = _stu_conv(phi, u, PADDED_SL)
            s = sigma ** SIGMA_POW
            out = jnp.einsum('btkd,k,kde->bte', U_plus, s, Mpp)
            out = out + jnp.einsum('btkd,k,kde->bte', U_minus, s, Mpm)
            return out

        def _compute_ar_u(Mu, u):
            sl = u.shape[1]
            out = jnp.zeros(u.shape[:2] + (Mu.shape[-1],), dtype=u.dtype)
            for i in range(Mu.shape[0]):
                ui = jnp.pad(u, ((0, 0), (i, 0), (0, 0)))[:, :sl]
                out = out + jnp.einsum('btd,de->bte', ui, Mu[i])
            return out

        def _stu(u, sigma, phi, Mu, Mpp, Mpm):
            return _compute_spectral(u, sigma, phi, Mpp, Mpm) + _compute_ar_u(Mu, u)
        key = jax.random.key(seed)
        ks = jax.random.split(key, 8)
        b, sl, d, K, k_u = (2, 4096, 128, 16, 3)
        x = jax.random.normal(ks[0], (b, sl, d), dtype=jnp.float32)
        sigma = jax.random.uniform(ks[1], (K,), dtype=jnp.float32, minval=0.001, maxval=1.0)
        phi = jax.random.normal(ks[2], (sl, K), dtype=jnp.float32) / np.sqrt(sl)
        M_u = jax.random.normal(ks[3], (4, k_u, d, d), dtype=jnp.float32) * 0.02
        M_phi_plus = jax.random.normal(ks[4], (4, K, d, d), dtype=jnp.float32) * 0.02
        M_phi_minus = jax.random.normal(ks[5], (4, K, d, d), dtype=jnp.float32) * 0.02
        log_weights = jnp.ones((4,), dtype=jnp.float32)
        u01 = jax.random.uniform(ks[6], (4,), dtype=jnp.float32, minval=1e-06, maxval=1.0 - 1e-06)
        gumbel = -jnp.log(-jnp.log(u01))
        return {'x': x, 'sigma': sigma, 'phi': phi, 'M_u': M_u, 'M_phi_plus': M_phi_plus, 'M_phi_minus': M_phi_minus, 'log_weights': log_weights, 'gumbel': gumbel}
    _L0_ffn_all = _L0_ffn_setup()
    _L0_ffn_in = {k: v for k, v in _L0_ffn_all.items() if k in ('sigma', 'phi', 'M_u', 'M_phi_plus', 'M_phi_minus', 'log_weights', 'gumbel', )}
    del _L0_ffn_all

    def _L1_conv_setup():
        import jax, jax.numpy as jnp
        from jax import lax
        import numpy as np
        B, C_IN, C_OUT, H, W, K = (16, 128, 128, 224, 224, 3)
        PAD = (K - 1) // 2

        def _make_cross_weights(c_out, c_in, k):
            w = jnp.zeros((c_out, c_in, k, k), dtype=jnp.float32)
            center = k // 2
            w = w.at[:, :, center, :].set(1.0)
            w = w.at[:, :, :, center].set(1.0)
            return w
        key = jax.random.key(seed)
        x = jax.random.normal(key, (B, C_IN, H, W), dtype=jnp.float32)
        weights = _make_cross_weights(C_OUT, C_IN, K)
        bias = jnp.zeros((C_OUT,), dtype=jnp.float32)
        return {'x': x, 'weights': weights, 'bias': bias}
    _L1_conv_all = _L1_conv_setup()
    _L1_conv_in = {k: v for k, v in _L1_conv_all.items() if k in ('weights', 'bias', )}
    del _L1_conv_all

    def _L1_ffn_setup():
        import jax, jax.numpy as jnp
        import numpy as np
        B, S, D, E, H, O, K = (512, 2048, 128, 64, 512, 128, 8)
        key = jax.random.key(seed)
        k0, k1, k2, k3 = jax.random.split(key, 4)
        x = jax.random.normal(k0, (B, S, D), dtype=jnp.float32)
        gate_w = jax.random.normal(k1, (E, D), dtype=jnp.float32) * (1.0 / np.sqrt(D))
        gate_b = jnp.zeros((E,), dtype=jnp.float32)
        weight1 = jax.random.uniform(k2, (E, D + 1, H), dtype=jnp.float32, minval=-1.0, maxval=1.0) * (1.0 / np.sqrt(D + 1))
        weight2 = jax.random.uniform(k3, (E, H + 1, O), dtype=jnp.float32, minval=-1.0, maxval=1.0) * (1.0 / np.sqrt(H + 1))
        return {'x': x, 'gate_w': gate_w, 'gate_b': gate_b, 'weight1': weight1, 'weight2': weight2}
    _L1_ffn_all = _L1_ffn_setup()
    _L1_ffn_in = {k: v for k, v in _L1_ffn_all.items() if k in ('gate_w', 'gate_b', 'weight1', 'weight2', )}
    del _L1_ffn_all

    return {
        "x": x,
        "L0_conv_W": _L0_conv_in["W"],
        "L0_ffn_sigma": _L0_ffn_in["sigma"],
        "L0_ffn_phi": _L0_ffn_in["phi"],
        "L0_ffn_M_u": _L0_ffn_in["M_u"],
        "L0_ffn_M_phi_plus": _L0_ffn_in["M_phi_plus"],
        "L0_ffn_M_phi_minus": _L0_ffn_in["M_phi_minus"],
        "L0_ffn_log_weights": _L0_ffn_in["log_weights"],
        "L0_ffn_gumbel": _L0_ffn_in["gumbel"],
        "L1_conv_weights": _L1_conv_in["weights"],
        "L1_conv_bias": _L1_conv_in["bias"],
        "L1_ffn_gate_w": _L1_ffn_in["gate_w"],
        "L1_ffn_gate_b": _L1_ffn_in["gate_b"],
        "L1_ffn_weight1": _L1_ffn_in["weight1"],
        "L1_ffn_weight2": _L1_ffn_in["weight2"],
    }

def reference(x, L0_conv_W, L0_ffn_sigma, L0_ffn_phi, L0_ffn_M_u, L0_ffn_M_phi_plus, L0_ffn_M_phi_minus, L0_ffn_log_weights, L0_ffn_gumbel, L1_conv_weights, L1_conv_bias, L1_ffn_gate_w, L1_ffn_gate_b, L1_ffn_weight1, L1_ffn_weight2):
    import jax
    import jax.numpy as jnp
    def _L0_conv_ref(x, W):
        import jax, jax.numpy as jnp
        import numpy as np
        B, C, H, W_SP = (16, 128, 28, 28)
        F, KS, STRIDE, PAD = (128, 3, 1, 1)
        CHUNK = 4
        EPS = 1e-12

        def _patches(x):
            p = jax.lax.conv_general_dilated_patches(x, (KS, KS), (STRIDE, STRIDE), [(PAD, PAD), (PAD, PAD)], dimension_numbers=('NCHW', 'OIHW', 'NCHW'))
            b, k, ho, wo = p.shape
            return (p.reshape(b, k, ho * wo), ho, wo)
        P, ho, wo = _patches(x)
        Wc = W.reshape(F, -1)
        K = Wc.shape[1]
        Wch = Wc.reshape(F // CHUNK, CHUNK, K)

        def chunk_fn(wc):
            return jnp.sum(jnp.abs(wc[None, :, :, None] - P[:, None, :, :]), axis=2)
        neg_l1 = -jax.lax.map(chunk_fn, Wch)
        neg_l1 = jnp.transpose(neg_l1, (1, 0, 2, 3)).reshape(P.shape[0], F, -1)
        d2 = jnp.sum(Wc * Wc, axis=1)[None, :, None] + jnp.sum(P * P, axis=1)[:, None, :] - 2.0 * jnp.einsum('fk,bkl->bfl', Wc, P)
        neg_l2 = -jnp.sqrt(jnp.maximum(d2, EPS))
        out = neg_l2 + jax.lax.stop_gradient(neg_l1 - neg_l2)
        return out.reshape(P.shape[0], F, ho, wo)

    def _L0_ffn_ref(x, sigma, phi, M_u, M_phi_plus, M_phi_minus, log_weights, gumbel):
        import jax, jax.numpy as jnp
        import numpy as np
        PADDED_SL = 8192
        TEMPERATURE = 1.0
        SIGMA_POW = 0.25

        def _stu_conv(phi, u, n):
            b, sl, d = u.shape
            sgn = jnp.where(jnp.arange(sl) % 2 == 0, 1.0, -1.0).astype(u.dtype)
            sgn3 = sgn[None, :, None]
            Vf = jnp.fft.rfft(phi, n=n, axis=0)
            Uf_p = jnp.fft.rfft(u, n=n, axis=1)
            Uf_m = jnp.fft.rfft(u * sgn3, n=n, axis=1)
            U_plus = jnp.fft.irfft(Vf[None, :, :, None] * Uf_p[:, :, None, :], n=n, axis=1)[:, :sl]
            U_minus = jnp.fft.irfft(Vf[None, :, :, None] * Uf_m[:, :, None, :], n=n, axis=1)[:, :sl]
            U_minus = U_minus * sgn[None, :, None, None]
            return (U_plus, U_minus)

        def _compute_spectral(u, sigma, phi, Mpp, Mpm):
            U_plus, U_minus = _stu_conv(phi, u, PADDED_SL)
            s = sigma ** SIGMA_POW
            out = jnp.einsum('btkd,k,kde->bte', U_plus, s, Mpp)
            out = out + jnp.einsum('btkd,k,kde->bte', U_minus, s, Mpm)
            return out

        def _compute_ar_u(Mu, u):
            sl = u.shape[1]
            out = jnp.zeros(u.shape[:2] + (Mu.shape[-1],), dtype=u.dtype)
            for i in range(Mu.shape[0]):
                ui = jnp.pad(u, ((0, 0), (i, 0), (0, 0)))[:, :sl]
                out = out + jnp.einsum('btd,de->bte', ui, Mu[i])
            return out

        def _stu(u, sigma, phi, Mu, Mpp, Mpm):
            return _compute_spectral(u, sigma, phi, Mpp, Mpm) + _compute_ar_u(Mu, u)
        T = x.shape[1]
        outs = []
        for i, frac in enumerate((1, 2, 4, 8)):
            xi = x[:, :T // frac]
            si = _stu(xi, sigma, phi, M_u[i], M_phi_plus[i], M_phi_minus[i])
            si = jnp.pad(si, ((0, 0), (0, T - si.shape[1]), (0, 0)))
            outs.append(si)
        y_soft = jax.nn.softmax((log_weights + gumbel) / TEMPERATURE)
        y_hard = jax.nn.one_hot(jnp.argmax(y_soft), 4, dtype=y_soft.dtype)
        weights = y_hard - jax.lax.stop_gradient(y_soft) + y_soft
        stacked = jnp.stack(outs, axis=-1)
        return jnp.sum(stacked * weights, axis=-1)

    def _L1_conv_ref(x, weights, bias):
        import jax, jax.numpy as jnp
        from jax import lax
        import numpy as np
        B, C_IN, C_OUT, H, W, K = (16, 128, 128, 224, 224, 3)
        PAD = (K - 1) // 2

        def _make_cross_weights(c_out, c_in, k):
            w = jnp.zeros((c_out, c_in, k, k), dtype=jnp.float32)
            center = k // 2
            w = w.at[:, :, center, :].set(1.0)
            w = w.at[:, :, :, center].set(1.0)
            return w
        out = lax.conv_general_dilated(x, weights, window_strides=(1, 1), padding=((PAD, PAD), (PAD, PAD)), dimension_numbers=('NCHW', 'OIHW', 'NCHW'))
        return out + bias[None, :, None, None]

    def _L1_ffn_ref(x, gate_w, gate_b, weight1, weight2):
        import jax, jax.numpy as jnp
        import numpy as np
        B, S, D, E, H, O, K = (512, 2048, 128, 64, 512, 128, 8)
        Bn, Sn, Dn = x.shape
        logits = jnp.einsum('bsd,ed->bse', x, gate_w) + gate_b
        probs = jax.nn.softmax(logits, axis=1)
        vals, idx = jax.lax.top_k(probs.transpose(0, 2, 1), K)
        topv = vals.transpose(0, 2, 1)
        topi = idx.transpose(0, 2, 1)
        flat_idx = topi.reshape(Bn, K * E)
        gathered = jnp.take_along_axis(x, flat_idx[:, :, None], axis=1)
        gathered = gathered.reshape(Bn, K, E, Dn)
        pooled = jnp.einsum('bked,bke->bed', gathered, topv)
        ones = jnp.ones((E, Bn, 1), dtype=x.dtype)
        h = jnp.concatenate([pooled.transpose(1, 0, 2), ones], axis=-1)
        h = jax.nn.gelu(jnp.einsum('ebd,edh->ebh', h, weight1), approximate=False)
        h = jnp.concatenate([h, ones], axis=-1)
        out = jnp.einsum('ebh,eho->ebo', h, weight2)
        out = out.transpose(1, 0, 2)
        weighted = jnp.einsum('beo,bke->bkeo', out, topv).reshape(Bn, K * E, O)
        outputs = jnp.zeros((Bn, Sn, O), dtype=x.dtype)
        outputs = outputs.at[jnp.arange(Bn)[:, None], flat_idx].add(weighted)
        return outputs

    def _gn(v, G=32, eps=1e-5):
        B_, C_, H_, W_ = v.shape
        g = v.reshape(B_, G, C_ // G, H_, W_)
        m = jnp.mean(g, axis=(2, 3, 4), keepdims=True)
        s = jnp.var(g, axis=(2, 3, 4), keepdims=True)
        return ((g - m) / jnp.sqrt(s + eps)).reshape(v.shape)

    def _ln_c(v, eps=1e-6):
        m = jnp.mean(v, axis=1, keepdims=True)
        s = jnp.var(v, axis=1, keepdims=True)
        return (v - m) / jnp.sqrt(s + eps)

    def _ln_t(v, eps=1e-5):
        m = jnp.mean(v, axis=-1, keepdims=True)
        s = jnp.var(v, axis=-1, keepdims=True)
        return (v - m) / jnp.sqrt(s + eps)

    def _to_tokens(v):
        B_, C_, H_, W_ = v.shape
        return v.reshape(B_, C_, H_ * W_).transpose(0, 2, 1)
    def _from_tokens(t, like):
        B_, C_, H_, W_ = like.shape
        return t.transpose(0, 2, 1).reshape(B_, C_, H_, W_)

    x = x + _L0_conv_ref(_ln_c(x), L0_conv_W)
    t = _to_tokens(x)
    t = t + _L0_ffn_ref(_ln_t(t), L0_ffn_sigma, L0_ffn_phi, L0_ffn_M_u, L0_ffn_M_phi_plus, L0_ffn_M_phi_minus, L0_ffn_log_weights, L0_ffn_gumbel)
    x = _from_tokens(t, x)
    x = x + _L1_conv_ref(_ln_c(x), L1_conv_weights, L1_conv_bias)
    t = _to_tokens(x)
    t = t + _L1_ffn_ref(_ln_t(t), L1_ffn_gate_w, L1_ffn_gate_b, L1_ffn_weight1, L1_ffn_weight2)
    x = _from_tokens(t, x)
    return x


_drawn_inputs = setup_inputs


def setup_inputs(seed=0):
    import zlib

    import numpy as np

    out = dict(_drawn_inputs(seed))
    spreads = {'L0_ffn_log_weights': (1.0, 0.2), 'L1_conv_bias': (0.0, 2.0), 'L1_ffn_gate_b': (0.0, 0.1)}
    factors = {'x': 6.94,
     'L0_conv_W': 8.0,
     'L0_ffn_sigma': 44.902,
     'L0_ffn_phi': 8.0,
     'L0_ffn_M_u': 64.0,
     'L0_ffn_M_phi_plus': 8.0,
     'L0_ffn_M_phi_minus': 8.0,
     'L0_ffn_gumbel': 8.0,
     'L1_conv_weights': 64.0,
     'L1_ffn_gate_w': 64.0,
     'L1_ffn_weight1': 64.0,
     'L1_ffn_weight2': 64.0}
    for name, (base, spread) in spreads.items():
        noise = np.random.default_rng([zlib.crc32(name.encode()), seed]).standard_normal(out[name].shape)
        drawn = base * np.exp(spread * noise) if base else spread * noise
        out[name] = jnp.asarray(drawn.astype(out[name].dtype))
    for name, factor in factors.items():
        out[name] = (out[name] * factor).astype(out[name].dtype)
    return out
```

```python
from contextlib import ExitStack

import concourse.bass as bass
from concourse import mybir

F32 = mybir.dt.float32
ALU = mybir.AluOpType
ACT = mybir.ActivationFunctionType
AX_X = mybir.AxisListType.X

B, C, H, W = 16, 128, 28, 28
T = H * W
HALF = T // 2
ROWS = H // 2
HP, WP = H + 2, W + 2
TAPS = 9
PAIRS = B // 2
TT = 112
NT = T // TT
STRIP = 98
STRIPS = T // STRIP
EPS_C, EPS_T = 1e-6, 1e-5

GROUPS = 4
PER_GROUP = C // GROUPS
SLOT_SETS = 4
PASS_TAPS = TAPS - 1
ACT_GROUPS = [(0, 1), (2, 3), (0, 1), (2, 3), (0, 1), (0, 1), (0, 1), (0,)]
LAST_TAP_AT = {1: 0, 3: 1, 5: 2, 7: 3}

N_OPT, K_F = 4, 16
N_LAG = 3
FRACS = (1, 2, 4, 8)
NF = T
FC = 56
NCH = NF // FC
F2 = 2 * FC
FCOLS = 2 * NF

E, HID, O = 64, 512, 128
HC = HID // 128
TOPK = 8
EG = 8


def dve_groups(tap):
    return sorted(set(range(GROUPS)) - set(ACT_GROUPS[tap]), key=lambda g: (g != LAST_TAP_AT.get(tap), g))


class Mem:

    def __init__(self, nc, ctx, tag):
        self.nc, self.ctx, self.tag, self.sems = nc, ctx, tag, []
        ctx.callback(self.end)

    def sb(self, name, shape, dt=F32):
        return self.ctx.enter_context(self.nc.sbuf_tensor(f"{self.tag}_{name}", shape, dt))

    def banks(self, name, n):
        return [self.ctx.enter_context(self.nc.psum_tensor(f"{self.tag}_{name}{i}", [128, 512], F32)) for i in range(n)]

    def end(self):
        if self.sems:
            self.nc.clear_and_free_semaphores(self.sems)
            self.nc.all_engine_barrier()

    def sem(self, name):
        self.sems.append(self.nc.alloc_semaphore(f"{self.tag}_{name}"))
        return self.sems[-1]


def phase_constants(nc, dram, const):
    with ExitStack() as ctx:
        m = Mem(nc, ctx, "cst")
        loaded, filled, cleared = m.sem("loaded"), m.sem("filled"), m.sem("cleared")
        block = ctx.enter_context(nc.Block())

        @block.sync
        def _(sp):
            sp.dma_start(const["ident"][:], dram["ident"]).then_inc(loaded, 16)

        @block.vector
        def _(dve):
            dve.memset(const["mean"][:], 1.0 / C).then_inc(filled, 1)
            dve.memset(const["ones"][:], 1.0).then_inc(filled, 1)
            dve.memset(const["eps"][:, 0:1], EPS_C).then_inc(filled, 1)
            dve.memset(const["eps"][:, 1:2], EPS_T).then_inc(filled, 1)
            dve.memset(const["gather"][:], 0.0).then_inc(cleared, 1)
            dve.wait_ge(cleared, 1)
            dve.memset(const["gather"][:, 31:32], 1.0 / C).then_inc(filled, 1)
            dve.wait_ge(loaded, 16)
            dve.tensor_copy(const["spread"][:], const["ident"][0:32, 0:STRIPS, None].to_broadcast([32, STRIPS, C])).then_inc(filled, 1)


def norm_pass(nc, tag, const, eps, inner, source, box=None, prepare=None):
    from_dram = isinstance(source, tuple)
    with ExitStack() as ctx:
        m = Mem(nc, ctx, tag)
        xr = m.sb("xr", [128, 2, 2, T]) if from_dram else None
        sq = m.sb("sq", [128, 2, T])
        sd = m.sb("sd", [32, 2, STRIP])
        stat = m.banks("stat", 4)
        var = m.banks("var", 2)
        mean_ok, centred, squared, var_ok, sd_ok, rs_ok, spread, normed = (
            m.sem(s) for s in ("mean_ok", "centred", "squared", "var_ok", "sd_ok", "rs_ok", "spread", "normed"))
        x_in = [m.sem("x_in0"), m.sem("x_in1")]
        if box:
            row3 = m.sb("row3", [128, 2, HP, W])
            base = m.sb("base", [128, 2, T])
            boxp = m.banks("box", 2)
            row2_ok, row3_ok, box_ok, base_ok, base_out, zeroed = (
                m.sem(s) for s in ("row2_ok", "row3_ok", "box_ok", "base_ok", "base_out", "zeroed"))
        else:
            zeroed = m.sem("zeroed")
        extra = prepare(m) if prepare else {}
        block = ctx.enter_context(nc.Block())

        def half_of_x(n, u, k, h):
            cols = slice(h * HALF, (h + 1) * HALF)
            flat = xr[:, u, k, cols] if from_dram else source[:, bass.ds(n + k, 1), cols].rearrange("p a t -> p (a t)")
            return flat

        @block.sync
        def _(sp):
            if from_dram:
                with sp.Fori(0, PAIRS // 2) as q:
                    for u in range(2):
                        sp.wait_ge(base_ok if box else centred, q * 4)
                        sp.dma_start(xr[:, u], source[0][:, bass.ds(q * 4 + 2 * u, 2), :]).then_inc(x_in[u], 16)

        @block.gpsimd
        def _(pool):
            if box:
                pool.memset(box[1][:], 0.0).then_inc(zeroed, 1)
                with pool.Fori(0, PAIRS) as p:
                    pool.wait_ge(base_ok, p * 2 + 2)
                    pool.dma_start(box[0]["base"][:, bass.ds(p * 2, 2), :], base[:]).then_inc(base_out, 16)
                pool.wait_ge(base_out, 16 * PAIRS)
            if "gpsimd" in extra:
                extra["gpsimd"](pool)

        @block.tensor
        def _(pe):
            with pe.Fori(0, PAIRS // 2) as q:
                for u in range(2):
                    n = q * 4 + 2 * u
                    if from_dram:
                        pe.wait_ge(x_in[u], q * 16 + 16)
                    for k in range(2):
                        if u:
                            pe.wait_ge(normed, n + k - 1)
                        else:
                            pe.wait_ge(normed, n)
                        for h in range(2):
                            mm = pe.matmul(stat[2 * k + h][:, 0:HALF], const["mean"][:], half_of_x(n, u, k, h),
                                           start=True, stop=True)
                        mm.then_inc(mean_ok, 1)
                    for k in range(2):
                        pe.wait_ge(sd_ok, n)
                        pe.wait_ge(squared, n + k + 1)
                        for j in range(STRIPS):
                            mm = pe.matmul(var[k][0:32, 0:STRIP], const["gather"][:, 31 - j:63 - j],
                                           sq[:, k, j * STRIP:(j + 1) * STRIP], start=(j == 0), stop=(j == STRIPS - 1))
                        mm.then_inc(var_ok, 1)
                    for k in range(2):
                        pe.wait_ge(rs_ok, n + k + 1)
                        for j in range(STRIPS):
                            c = (j % 4) * STRIP
                            mm = pe.matmul(stat[2 * k + j // 4][:, c:c + STRIP], const["spread"][:, j, :], sd[:, k],
                                           start=True, stop=True)
                        mm.then_inc(spread, 1)
                    if box:
                        for k in range(2):
                            pe.wait_ge(base_ok, n + k)
                            pe.wait_ge(row3_ok, n + k + 1)
                            for h in range(2):
                                for dy in range(3):
                                    mm = pe.matmul(boxp[h][:, 0:HALF], const["ones"][:, 0:128],
                                                   row3[:, k, h * ROWS + dy:h * ROWS + dy + ROWS, :],
                                                   start=(dy == 0), stop=(dy == 2))
                            mm.then_inc(box_ok, 1)
            if "tensor" in extra:
                extra["tensor"](pe, var[0])

        @block.scalar
        def _(act):
            with act.Fori(0, PAIRS) as p:
                for k in range(2):
                    act.wait_ge(centred, p * 2 + k + 1)
                    act.wait_ge(var_ok, p * 2)
                    for h in range(2):
                        a = act.activation(sq[:, k, h * HALF:(h + 1) * HALF].rearrange("p (h w) -> p h w", w=W),
                                           inner(p * 2 + k, h), ACT.Square)
                    a.then_inc(squared, 1)
                for k in range(2):
                    act.wait_ge(var_ok, p * 2 + k + 1)
                    act.wait_ge(spread, p * 2)
                    act.activation(sd[:, k], var[k][0:32, 0:STRIP], ACT.Sqrt, bias=const["eps"][0:32, eps:eps + 1])\
                       .then_inc(sd_ok, 1)

        @block.vector
        def _(dve):
            if box:
                dve.wait_ge(zeroed, 1)
            with dve.Fori(0, PAIRS // 2) as q:
                for u in range(2):
                    n = q * 4 + 2 * u
                    for k in range(2):
                        dve.wait_ge(mean_ok, n + k + 1)
                        for h in range(2):
                            v = dve.tensor_tensor(
                                inner(n + k, h), half_of_x(n, u, k, h).rearrange("p (h w) -> p h w", w=W),
                                stat[2 * k + h][:, 0:HALF].rearrange("p (h w) -> p h w", w=W), ALU.subtract)
                        v.then_inc(centred, 1)
                    for k in range(2):
                        dve.wait_ge(sd_ok, n + k + 1)
                        dve.reciprocal(sd[:, k], sd[:, k]).then_inc(rs_ok, 1)
                    for k in range(2):
                        dve.wait_ge(spread, n + k + 1)
                        for h in range(2):
                            v = dve.tensor_tensor(inner(n + k, h), inner(n + k, h),
                                                  stat[2 * k + h][:, 0:HALF].rearrange("p (h w) -> p h w", w=W), ALU.mult)
                        v.then_inc(normed, 1)
                    if box:
                        image = [box[1][:, bass.ds(n + k, 1)].rearrange("p a h w -> p (a h) w") for k in range(2)]
                        dve.wait_ge(box_ok, n)
                        for k in range(2):
                            dve.wait_ge(normed, n + k + 1)
                            dve.tensor_tensor(row3[:, k], image[k][:, :, 0:W], image[k][:, :, 1:W + 1], ALU.add)\
                               .then_inc(row2_ok, 1)
                        for k in range(2):
                            dve.wait_ge(row2_ok, n + k + 1)
                            dve.tensor_tensor(row3[:, k], row3[:, k], image[k][:, :, 2:W + 2], ALU.add).then_inc(row3_ok, 1)
                        dve.wait_ge(base_out, n * 8)
                        for k in range(2):
                            dve.wait_ge(box_ok, n + k + 1)
                            for h in range(2):
                                v = dve.tensor_tensor(base[:, k, h * HALF:(h + 1) * HALF], boxp[h][:, 0:HALF],
                                                      half_of_x(n, u, k, h), ALU.add)
                            v.then_inc(base_ok, 1)
            if "vector" in extra:
                extra["vector"](dve)


def weight_tables(nc, dram, wt):
    with ExitStack() as ctx:
        m = Mem(nc, ctx, "aw")
        signed = m.sb("signed", [128, PER_GROUP, TAPS, GROUPS])
        w_in, signs_ok, signed_ok, tables_ok = (m.sem(s) for s in ("w_in", "signs_ok", "signed_ok", "tables_ok"))
        block = ctx.enter_context(nc.Block())

        @block.sync
        def _(sp):
            sp.dma_start(wt["w"][:], dram["w0"]).then_inc(w_in, 16)

        @block.vector
        def _(dve):
            dve.memset(signed[:], 1.0).then_inc(signs_ok, 1)
            dve.wait_ge(signs_ok, 1)
            for tap in range(PASS_TAPS):
                for g in ACT_GROUPS[tap]:
                    v = dve.memset(signed[:, :, tap, g], -1.0)
            v.then_inc(signs_ok, 1)
            dve.memset(wt["selectors"][:], 0.0).then_inc(tables_ok, 1)
            dve.wait_ge(tables_ok, 1)
            dve.memset(wt["selectors"][:, 0:PER_GROUP * PER_GROUP:PER_GROUP + 1], -2.0)
            dve.wait_ge(signs_ok, 2)
            dve.wait_ge(w_in, 16)
            dve.tensor_tensor(signed[:], signed[:], wt["w"][:], ALU.mult).then_inc(signed_ok, 1)
            dve.tensor_scalar(wt["neg"][:], wt["w"][:], -1.0, None, ALU.mult)
            dve.wait_ge(signed_ok, 1)
            for g in range(GROUPS):
                dve.tensor_reduce(wt["signed_sum"][:, g * PER_GROUP:(g + 1) * PER_GROUP], signed[:, :, :, g], AX_X, ALU.add)


def phase_distance(nc, dram, const, xpad, wt):
    BODY_J = 2
    JJ = PER_GROUP // BODY_J
    SETS = PASS_TAPS * BODY_J
    ACTS = sum(map(len, ACT_GROUPS))
    DVES = PASS_TAPS * GROUPS - ACTS + GROUPS
    with ExitStack() as ctx:
        m = Mem(nc, ctx, "ad")
        diff = m.sb("diff", [128, SLOT_SETS, GROUPS, 2, H, W])
        sel = m.sb("sel", [128, BODY_J, PER_GROUP])
        base = m.sb("base", [128, 2, T])
        out = m.sb("out", [128, 2, T])
        acc = m.banks("acc", 4)
        sel_ok, act_tile, dve_tile, set_free = (m.sem(s) for s in ("sel_ok", "act_tile", "dve_tile", "set_free"))
        pair_summed, pair_taken, base_in, base_used, x_out = (
            m.sem(s) for s in ("pair_summed", "pair_taken", "base_in", "base_used", "x_out"))
        block = ctx.enter_context(nc.Block())

        def window(p, tap):
            dy, dx = divmod(tap, 3)
            return xpad[:, bass.ds(p * 2, 2), dy:dy + H, dx:dx + W]

        @block.sync
        def _(sp):
            with sp.Fori(0, PAIRS) as p:
                sp.wait_ge(base_used, p)
                sp.dma_start(base[:], dram["base"][:, bass.ds(p * 2, 2), :]).then_inc(base_in, 16)
                sp.wait_ge(pair_taken, p + 1)
                sp.dma_start(dram["x1"][:, bass.ds(p * 2, 2), :], out[:]).then_inc(x_out, 16)
            sp.wait_ge(x_out, 16 * PAIRS)

        @block.gpsimd
        def _(pool):
            for s in range(SLOT_SETS):
                pool.memset(diff[:, s], 0.0).then_inc(set_free, 1)
            with pool.Fori(0, PAIRS) as p:
                with pool.Fori(0, JJ) as jj:
                    n = (p * JJ + jj)
                    for jb in range(BODY_J):
                        pool.wait_ge(set_free, n * SETS + jb * SLOT_SETS)
                        pool.tensor_copy(sel[:, jb], wt["selectors"][:, bass.ds((jj * BODY_J + jb) * PER_GROUP, PER_GROUP)])\
                            .then_inc(sel_ok, 1)

        @block.scalar
        def _(act):
            with act.Fori(0, PAIRS) as p:
                with act.Fori(0, JJ) as jj:
                    n = (p * JJ + jj) * SETS
                    for jb in range(BODY_J):
                        for tap in range(PASS_TAPS):
                            act.wait_ge(set_free, n + jb * PASS_TAPS + tap + 1)
                            for g in ACT_GROUPS[tap]:
                                act.activation(diff[:, tap % SLOT_SETS, g], window(p, tap), ACT.Relu,
                                               bias=wt["neg"][:, bass.ds(jj * BODY_J + jb, 1), tap, g]).then_inc(act_tile, 1)

        @block.vector
        def _(dve):
            def weight(jj, jb, tap, g):
                return wt["w"][:, bass.ds(jj * BODY_J + jb, 1), tap, g]

            def last_tap(p, jj, jb, tap, g):
                dy, dx = divmod(TAPS - 1, 3)
                for b in range(2):
                    tile = diff[:, tap % SLOT_SETS, g, b]
                    v = dve.scalar_tensor_tensor(
                        tile, xpad[:, bass.ds(p * 2 + b, 1), dy:dy + H, dx:dx + W].rearrange("p a h w -> p (a h) w"),
                        weight(jj, jb, TAPS - 1, g), tile, ALU.max, ALU.add)
                v.then_inc(dve_tile, 1)

            with dve.Fori(0, PAIRS) as p:
                with dve.Fori(0, JJ) as jj:
                    n = p * JJ + jj
                    for jb in range(BODY_J):
                        done = 0
                        for tap in range(PASS_TAPS):
                            dve.wait_ge(set_free, n * SETS + jb * PASS_TAPS + tap + 1)
                            for g in dve_groups(tap):
                                dve.tensor_scalar(diff[:, tap % SLOT_SETS, g], window(p, tap), weight(jj, jb, tap, g), None,
                                                  ALU.max).then_inc(dve_tile, 1)
                            if tap in LAST_TAP_AT:
                                dve.wait_ge(dve_tile, n * (BODY_J * DVES) + jb * DVES + done + 1)
                                last_tap(p, jj, jb, tap, LAST_TAP_AT[tap])
                                done += 1
                            done += len(dve_groups(tap))
                dve.wait_ge(pair_summed, p + 1)
                dve.wait_ge(x_out, p * 16)
                for q in range(4):
                    v = dve.tensor_copy(out[:, q // 2, (q % 2) * HALF:(q % 2 + 1) * HALF], acc[q][:, 0:HALF])
                v.then_inc(pair_taken, 1)

        @block.tensor
        def _(pe):
            with pe.Fori(0, PAIRS) as p:
                pe.wait_ge(pair_taken, p)
                pe.wait_ge(base_in, p * 16 + 16)
                for q in range(4):
                    mm = pe.matmul(acc[q][:, 0:HALF], const["ident"][:], base[:, q // 2, (q % 2) * HALF:(q % 2 + 1) * HALF],
                                   start=True, stop=False, skip_group_check=True)
                mm.then_inc(base_used, 1)
                with pe.Fori(0, JJ) as jj:
                    n = p * JJ + jj
                    for jb in range(BODY_J):
                        pe.wait_ge(sel_ok, n * BODY_J + jb + 1)
                        acts, dves = 0, 0
                        for tap in range(PASS_TAPS):
                            acts += len(ACT_GROUPS[tap])
                            dves += len(dve_groups(tap)) + (tap in LAST_TAP_AT)
                            pe.wait_ge(act_tile, n * (BODY_J * ACTS) + jb * ACTS + acts)
                            pe.wait_ge(dve_tile, n * (BODY_J * DVES) + jb * DVES + dves)
                            for q in range(4):
                                for g in range(GROUPS):
                                    mm = pe.matmul(acc[q][32 * g:32 * (g + 1), 0:HALF], sel[:, jb],
                                                   diff[:, tap % SLOT_SETS, g, q // 2, (q % 2) * ROWS:(q % 2 + 1) * ROWS, :],
                                                   start=False, stop=False, skip_group_check=True)
                            mm.then_inc(set_free, 1)
                for q in range(4):
                    mm = pe.matmul(acc[q][:, 0:HALF], wt["signed_sum"][:], wt["ones"][:, 0:HALF], start=False, stop=True,
                                   skip_group_check=True)
                mm.then_inc(pair_summed, 1)


def layer0_distance(nc, dram, const):
    with ExitStack() as ctx:
        m = Mem(nc, ctx, "a")
        xpad = m.sb("xpad", [128, B, HP, WP])
        wt = {"w": m.sb("w", [128, PER_GROUP, TAPS, GROUPS]), "neg": m.sb("neg", [128, PER_GROUP, TAPS, GROUPS]),
              "signed_sum": m.sb("signed_sum", [128, C]), "selectors": m.sb("selectors", [128, PER_GROUP * PER_GROUP]),
              "ones": const["ones"]}

        def inner(b, h):
            return xpad[:, bass.ds(b, 1), 1 + ROWS * h:1 + ROWS * (h + 1), 1:W + 1].rearrange("p a h w -> p (a h) w")

        weight_tables(nc, dram, wt)
        norm_pass(nc, "an", const, 0, inner, (dram["x"],), box=(dram, xpad))
        phase_distance(nc, dram, const, xpad, wt)


def operator_gates(nc, dram, const, sp_):
    with ExitStack() as ctx:
        m = Mem(nc, ctx, "bg")
        logw = m.sb("logw", [128, N_OPT])
        gum = m.sb("gum", [128, N_OPT])
        own = m.sb("own", [128, N_OPT])
        sig = m.sb("sig", [128, 1])
        soft = m.sb("soft", [128, N_OPT])
        col = m.sb("col", [128, 8])
        same = m.sb("same", [128, N_OPT])
        hard = m.sb("hard", [128, N_OPT])
        wts = m.sb("wts", [128, N_OPT])
        mu = m.sb("mu", [128, N_OPT, N_LAG, C])
        phi = m.sb("phi", [TT, NT, K_F])
        sgn = m.sb("sgn", [TT, 1])
        filt = m.sb("filt", [TT, NT, N_OPT, 2, K_F])
        fp = m.banks("fp", 4)
        small_in, mu_in, phi_in, exp_ok, sig_ok, filt_ok, hat_ok, hat_taken, step = (
            m.sem(s) for s in ("small_in", "mu_in", "phi_in", "exp_ok", "sig_ok", "filt_ok", "hat_ok", "hat_taken", "step"))
        neg_ok, dft_in = m.sem("neg_ok"), m.sem("dft_in")
        block = ctx.enter_context(nc.Block())

        @block.sync
        def _(sp):
            for dst, name in ((logw, "log_weights"), (gum, "gumbel"), (own, "own"), (sig, "sigma")):
                sp.dma_start(dst[:], dram[name]).then_inc(small_in, 16)
            sp.dma_start(phi[:], dram["phi"]).then_inc(phi_in, 16)
            sp.dma_start(sgn[:], dram["sgn"]).then_inc(phi_in, 16)
            sp.dma_start(sp_["dft"][:], dram["dft"]).then_inc(dft_in, 16)
            sp.dma_start(mu[:], dram["mu"]).then_inc(mu_in, 16)

        @block.scalar
        def _(act):
            act.wait_ge(neg_ok, 1)
            act.activation(soft[:], soft[:], ACT.Exp, bias=col[:, 1:2]).then_inc(exp_ok, 1)
            act.activation(sig[:], sig[:], ACT.Sqrt).then_inc(sig_ok, 1)
            act.wait_ge(sig_ok, 1)
            act.activation(sig[:], sig[:], ACT.Sqrt).then_inc(sig_ok, 1)

        @block.tensor
        def _(pe):
            pe.wait_ge(filt_ok, 1)
            pe.wait_ge(dft_in, 16)
            for c in range(4):
                for i in range(NT):
                    mm = pe.matmul(fp[c][:, 0:HALF], filt[:, i].rearrange("p a b k -> p (a b k)"),
                                   sp_["dft"][:, i, c * HALF:(c + 1) * HALF], start=(i == 0), stop=(i == NT - 1))
                mm.then_inc(hat_ok, 1)

        @block.vector
        def _(dve):
            count = [0]

            def then(ins):
                count[0] += 1
                ins.then_inc(step, 1)
                dve.wait_ge(step, count[0])

            dve.wait_ge(small_in, 64)
            dve.wait_ge(phi_in, 32)
            for i in range(N_OPT):
                dve.tensor_copy(filt[:, :, i, 0, :], phi[:])
                v = dve.tensor_scalar(filt[:, :, i, 1, :], phi[:], sgn[:, 0:1], None, ALU.mult)
            v.then_inc(filt_ok, 1)
            then(dve.tensor_tensor(soft[:], logw[:], gum[:], ALU.add))
            then(dve.tensor_reduce(col[:, 0:1], soft[:], AX_X, ALU.max))
            dve.tensor_scalar(col[:, 1:2], col[:, 0:1], -1.0, None, ALU.mult).then_inc(neg_ok, 1)
            dve.wait_ge(exp_ok, 1)
            then(dve.tensor_reduce(col[:, 2:3], soft[:], AX_X, ALU.add))
            then(dve.reciprocal(col[:, 3:4], col[:, 2:3]))
            then(dve.tensor_scalar(soft[:], soft[:], col[:, 3:4], None, ALU.mult))
            then(dve.tensor_reduce(col[:, 4:5], soft[:], AX_X, ALU.max))
            then(dve.tensor_scalar(same[:], soft[:], col[:, 4:5], None, ALU.is_ge))
            then(dve.memset(col[:, 5:6], 1.0))
            for i in range(N_OPT):
                then(dve.tensor_tensor(hard[:, i:i + 1], same[:, i:i + 1], col[:, 5:6], ALU.mult))
                then(dve.tensor_tensor(col[:, 5:6], col[:, 5:6], hard[:, i:i + 1], ALU.subtract))
            then(dve.tensor_tensor(wts[:], hard[:], soft[:], ALU.subtract))
            then(dve.tensor_tensor(wts[:], wts[:], soft[:], ALU.add))
            lo = 0
            for i in reversed(range(N_OPT)):
                hi = T // FRACS[i]
                then(dve.tensor_reduce(col[:, 6:7], hard[:, 0:i + 1], AX_X, ALU.add))
                then(dve.tensor_scalar(sp_["mask"][:, lo:hi], const["ones"][:, 0:hi - lo], col[:, 6:7], None, ALU.mult))
                lo = hi
            dve.wait_ge(mu_in, 16)
            muw = sp_["muw"][:].rearrange("p s e -> p (s e)")
            then(dve.tensor_scalar(muw, mu[:, 0].rearrange("p s e -> p (s e)"), wts[:, 0:1], None, ALU.mult))
            for i in range(1, N_OPT):
                then(dve.scalar_tensor_tensor(muw, mu[:, i].rearrange("p s e -> p (s e)"), wts[:, i:i + 1], muw,
                                              ALU.mult, ALU.add))
            then(dve.tensor_tensor(own[:], own[:], wts[:], ALU.mult))
            then(dve.tensor_reduce(col[:, 7:8], own[:], AX_X, ALU.add))
            dve.wait_ge(sig_ok, 2)
            then(dve.tensor_tensor(col[:, 7:8], col[:, 7:8], sig[:], ALU.mult))
            for c in range(4):
                dve.wait_ge(hat_ok, c + 1)
                dve.tensor_scalar(sp_["hat"][:, c * HALF:(c + 1) * HALF], fp[c][:, 0:HALF], col[:, 7:8], None, ALU.mult)


def spectral_forward(nc, dram, const, sp_, u):
    with ExitStack() as ctx:
        m = Mem(nc, ctx, "bf")
        us = m.sb("us", [128, 2, N_LAG - 1 + T])
        ut = m.sb("ut", [TT, 2, NT, C])
        uh = m.sb("uh", [128, 2, FCOLS])
        xr = m.sb("xr", [128, 2, T])
        ar = m.sb("ar", [128, 2, T])
        turned = m.banks("turned", 2)
        arp = m.banks("arp", 2)
        fwd = m.banks("fwd", 4)
        staged, turn_ok, turn_taken, ar_ok, ar_masked, ar_added, padded = (
            m.sem(s) for s in ("staged", "turn_ok", "turn_taken", "ar_ok", "ar_masked", "ar_added", "padded"))
        fwd_ok, fwd_act, fwd_dve = m.sem("fwd_ok"), m.sem("fwd_act"), m.sem("fwd_dve")
        x_in = [m.sem("x_in0"), m.sem("x_in1")]
        x_out = [m.sem("x_out0"), m.sem("x_out1")]
        uh_out = [m.sem("uh_out0"), m.sem("uh_out1")]
        PAD = N_LAG - 1
        block = ctx.enter_context(nc.Block())

        @block.sync
        def _(sp):
            with sp.Fori(0, PAIRS) as p:
                for k in range(2):
                    sp.wait_ge(x_out[k], p * 16)
                    sp.dma_start(xr[:, k], dram["x1"][:, bass.ds(p * 2 + k, 1), :].rearrange("c b t -> c (b t)")).then_inc(x_in[k], 16)
                for k in range(2):
                    sp.wait_ge(ar_added, p * 2 + k + 1)
                    sp.dma_start(dram["x1b"][:, bass.ds(p * 2 + k, 1), :].rearrange("c b t -> c (b t)"), xr[:, k]).then_inc(x_out[k], 16)
                for k in range(2):
                    sp.wait_ge(fwd_act, p * 4 + 2 * k + 2)
                    sp.wait_ge(fwd_dve, p * 4 + 2 * k + 2)
                    sp.dma_start(dram["uhat"][:, :, bass.ds(p * 2 + k, 1), :].rearrange("n c b f -> c n (b f)"),
                                 uh[:, k].rearrange("c (n f) -> c n f", f=F2)).then_inc(uh_out[k], 16)
            for k in range(2):
                sp.wait_ge(x_out[k], 16 * PAIRS)
                sp.wait_ge(uh_out[k], 16 * PAIRS)

        @block.gpsimd
        def _(pool):
            for k in range(2):
                pool.memset(us[:, k, 0:PAD], 0.0).then_inc(padded, 1)
            with pool.Fori(0, PAIRS) as p:
                for k in range(2):
                    pool.wait_ge(ar_ok, p * 2)
                    pool.tensor_copy(us[:, k, PAD:PAD + T], u[:, bass.ds(p * 2 + k, 1), :].rearrange("p a t -> p (a t)"))\
                        .then_inc(staged, 1)

        @block.tensor
        def _(pe):
            pe.wait_ge(padded, 2)
            with pe.Fori(0, PAIRS) as p:
                for k in range(2):
                    pe.wait_ge(staged, p * 2 + k + 1)
                    pe.wait_ge(turn_taken, p * 2 + k)
                    for i in range(NT):
                        mm = pe.transpose(turned[i // 4][0:TT, (i % 4) * C:(i % 4 + 1) * C],
                                          us[:, k, PAD + i * TT:PAD + (i + 1) * TT], const["ident"][:])
                    mm.then_inc(turn_ok, 1)
                    pe.wait_ge(ar_masked, p * 2 + k)
                    for h in range(2):
                        for s in range(N_LAG):
                            mm = pe.matmul(arp[h][:, 0:HALF], sp_["muw"][:, s, :],
                                           us[:, k, PAD - s + h * HALF:PAD - s + (h + 1) * HALF],
                                           start=(s == 0), stop=(s == N_LAG - 1))
                    mm.then_inc(ar_ok, 1)
                for k in range(2):
                    pe.wait_ge(turn_taken, p * 2 + k + 1)
                    for c in range(4):
                        pe.wait_ge(fwd_dve if c % 2 else fwd_act, p * 4 + (2 * k + c // 2 - 1 if k else 0))
                        for i in range(NT):
                            mm = pe.matmul(fwd[c][:, 0:HALF], ut[:, k, i], sp_["dft"][:, i, c * HALF:(c + 1) * HALF],
                                           start=(i == 0), stop=(i == NT - 1))
                        mm.then_inc(fwd_ok, 1)

        @block.scalar
        def _(act):
            with act.Fori(0, PAIRS) as p:
                for k in range(2):
                    act.wait_ge(turn_ok, p * 2 + k + 1)
                    act.wait_ge(fwd_ok, p * 8)
                    act.activation(ut[:, k, 0:4].rearrange("p i c -> p (i c)"), turned[0][0:TT, :], ACT.Copy)
                    act.activation(ut[:, k, 4:NT].rearrange("p i c -> p (i c)"), turned[1][0:TT, 0:(NT - 4) * C], ACT.Copy)\
                       .then_inc(turn_taken, 1)
                for k in range(2):
                    act.wait_ge(uh_out[k], p * 16)
                    for c in (0, 2):
                        act.wait_ge(fwd_ok, p * 8 + 4 * k + c + 1)
                        act.activation(uh[:, k, c * HALF:(c + 1) * HALF], fwd[c][:, 0:HALF], ACT.Copy).then_inc(fwd_act, 1)

        @block.vector
        def _(dve):
            with dve.Fori(0, PAIRS) as p:
                for k in range(2):
                    dve.wait_ge(ar_ok, p * 2 + k + 1)
                    for h in range(2):
                        v = dve.tensor_tensor(ar[:, k, h * HALF:(h + 1) * HALF], arp[h][:, 0:HALF],
                                              sp_["mask"][:, h * HALF:(h + 1) * HALF], ALU.mult)
                    v.then_inc(ar_masked, 1)
                for k in range(2):
                    dve.wait_ge(ar_masked, p * 2 + k + 1)
                    dve.wait_ge(x_in[k], p * 16 + 16)
                    dve.tensor_tensor(xr[:, k], xr[:, k], ar[:, k], ALU.add).then_inc(ar_added, 1)
                for k in range(2):
                    dve.wait_ge(uh_out[k], p * 16)
                    for c in (1, 3):
                        dve.wait_ge(fwd_ok, p * 8 + 4 * k + c + 1)
                        dve.tensor_copy(uh[:, k, c * HALF:(c + 1) * HALF], fwd[c][:, 0:HALF]).then_inc(fwd_dve, 1)


def spectral_apply(nc, dram, const, sp_):
    EQ = 4
    NQ = C // EQ
    FB = 16
    with ExitStack() as ctx:
        m = Mem(nc, ctx, "bm")
        mat = m.sb("mat", [128, C, C])
        gf = m.sb("gf", [128, F2, C])
        uc = m.sb("uc", [128, B, F2])
        ui = m.sb("ui", [128, B, 2, FC])
        yc = m.sb("yc", [128, B, F2])
        yt = m.sb("yt", [F2, 2, B, C])
        gp = m.banks("gp", 4)
        yp = m.banks("yp", 2)
        tp = m.banks("tp", 2)
        MAT_PARTS = 8
        mat_in = [m.sem(f"mat_in{i}") for i in range(MAT_PARTS)]
        uc_in, ui_ok, g_made, g_act, g_dve, y_made, y_act, y_dve, t_made, t_act, t_dve = (
            m.sem(s) for s in ("uc_in", "ui_ok", "g_made", "g_act", "g_dve", "y_made", "y_act", "y_dve", "t_made", "t_act", "t_dve"))
        yt_out = [m.sem("yt_out0"), m.sem("yt_out1")]
        YQ = -(-FC // FB)
        PE_T = B // 4
        block = ctx.enter_context(nc.Block())

        @block.sync
        def _(sp):
            with sp.Fori(0, NCH) as n:
                sp.wait_ge(y_made, n * YQ)
                sp.dma_start(uc[:], dram["uhat"][bass.ds(n, 1)].rearrange("n c b f -> c (n b) f")).then_inc(uc_in, 16)

        @block.gpsimd
        def _(pool):
            step = C // MAT_PARTS
            for i in range(MAT_PARTS):
                pool.dma_start(mat[:, i * step:(i + 1) * step], dram["mat"][:, i * step:(i + 1) * step]).then_inc(mat_in[i], 16)
            with pool.Fori(0, NCH // 2) as nn:
                for v in range(2):
                    pool.wait_ge(t_act, (nn * 2 + v + 1) * (PE_T // 2))
                    pool.wait_ge(t_dve, (nn * 2 + v + 1) * (PE_T // 2))
                    pool.dma_start(dram["yt"][bass.ds(nn * 2 + v, 1)].rearrange("n f b c -> f (n b) c"), yt[:, v]).then_inc(yt_out[v], 16)
            for v in range(2):
                pool.wait_ge(yt_out[v], 16 * (NCH // 2))

        @block.tensor
        def _(pe):
            for i in range(MAT_PARTS):
                pe.wait_ge(mat_in[i], 16)
            with pe.Fori(0, NCH) as n:
                for q in range(NQ):
                    done, taken = (n * (NQ // 2), g_dve if q % 2 else g_act)
                    pe.wait_ge(taken, done + (q // 2 - 1 if q >= 4 else 0))
                    for e in range(EQ):
                        mm = pe.matmul(gp[q % 4][:, e * F2:(e + 1) * F2], mat[:, q * EQ + e], sp_["hat"][:, bass.ds(n * F2, F2)],
                                       start=True, stop=True)
                    mm.then_inc(g_made, 1)
                pe.wait_ge(g_act, (n + 1) * (NQ // 2))
                pe.wait_ge(g_dve, (n + 1) * (NQ // 2))
                pe.wait_ge(uc_in, n * 16 + 16)
                pe.wait_ge(ui_ok, n * 2 + 2)
                for y in range(YQ):
                    pe.wait_ge(y_dve if y % 2 else y_act, n * (YQ // 2) + y // 2)
                    for f in range(y * FB, min((y + 1) * FB, FC)):
                        at = (f - y * FB) * 2 * B
                        res = yp[y % 2][:, at:at + 2 * B]
                        pe.matmul(res, gf[:, f], uc[:, :, f:f + FC + 1:FC], start=True, stop=False)
                        mm = pe.matmul(res, gf[:, FC + f], ui[:, :, :, f], start=False, stop=True)
                    mm.then_inc(y_made, 1)
                pe.wait_ge(y_act, (n + 1) * (YQ // 2))
                pe.wait_ge(y_dve, (n + 1) * (YQ // 2))
                for t in range(PE_T):
                    pe.wait_ge(t_dve if t % 2 else t_act, n * (PE_T // 2) + t // 2)
                    for b in range(4):
                        mm = pe.transpose(tp[t % 2][0:F2, b * C:(b + 1) * C], yc[:, t * 4 + b, :], const["ident"][:])
                    mm.then_inc(t_made, 1)

        def take(eng, copy, n, v, mine, g_taken, y_taken, t_taken):
            for q in range(mine, NQ, 2):
                if q == mine:
                    eng.wait_ge(y_made, n * YQ)
                eng.wait_ge(g_made, n * NQ + q + 1)
                copy(gf[:, :, q * EQ:(q + 1) * EQ].rearrange("p f e -> p e f"),
                     gp[q % 4][:, 0:EQ * F2].rearrange("p (e f) -> p e f", e=EQ)).then_inc(g_taken, 1)
            for y in range(mine, YQ, 2):
                if y == mine:
                    eng.wait_ge(t_made, n * PE_T)
                eng.wait_ge(y_made, n * YQ + y + 1)
                k = min(FB, FC - y * FB)
                copy(yc[:].rearrange("p b (r f) -> p f b r", r=2)[:, y * FB:y * FB + k],
                     yp[y % 2][:, 0:k * 2 * B].rearrange("p (f b r) -> p f b r", b=B, r=2)).then_inc(y_taken, 1)
            for t in range(mine, PE_T, 2):
                if t == mine:
                    eng.wait_ge(yt_out[v], (n - v) * 8)
                eng.wait_ge(t_made, n * PE_T + t + 1)
                copy(yt[:, v, t * 4:(t + 1) * 4].rearrange("p b c -> p (b c)"), tp[t % 2][0:F2, :]).then_inc(t_taken, 1)

        @block.scalar
        def _(act):
            with act.Fori(0, NCH // 2) as nn:
                for v in range(2):
                    n = nn * 2 + v
                    act.wait_ge(uc_in, n * 16 + 16)
                    act.wait_ge(y_made, n * YQ)
                    act.activation(ui[:, :, 0], uc[:, :, FC:F2], ACT.Copy, scale=-1.0).then_inc(ui_ok, 1)
                    act.activation(ui[:, :, 1], uc[:, :, 0:FC], ACT.Copy).then_inc(ui_ok, 1)
                    take(act, lambda o, i: act.activation(o, i, ACT.Copy), n, v, 0, g_act, y_act, t_act)

        @block.vector
        def _(dve):
            with dve.Fori(0, NCH // 2) as nn:
                for v in range(2):
                    take(dve, dve.tensor_copy, nn * 2 + v, v, 1, g_dve, y_dve, t_dve)


def spectral_inverse(nc, dram, const, sp_, x):
    with ExitStack() as ctx:
        m = Mem(nc, ctx, "bi")
        idft = m.sb("idft", [F2, NCH, T])
        yt = m.sb("yt", [F2, 2, NCH, C])
        part = m.sb("part", [128, 2, T])
        inv = m.banks("inv", 4)
        idft_in, x_in, inv_ok, masked, added = (m.sem(s) for s in ("idft_in", "x_in", "inv_ok", "masked", "added"))
        yt_in = [m.sem("yt_in0"), m.sem("yt_in1")]
        block = ctx.enter_context(nc.Block())

        @block.sync
        def _(sp):
            with sp.Fori(0, PAIRS) as p:
                for k in range(2):
                    sp.wait_ge(inv_ok, p * 2)
                    sp.dma_start(yt[:, k], dram["yt"][:, :, bass.ds(p * 2 + k, 1), :].rearrange("n f b c -> f n (b c)"))\
                      .then_inc(yt_in[k], 16)

        @block.gpsimd
        def _(pool):
            pool.dma_start(idft[:], dram["idft"]).then_inc(idft_in, 16)
            pool.dma_start(x[:, 0:2 * PAIRS], dram["x1b"][:, 0:2 * PAIRS]).then_inc(x_in, 16)

        @block.tensor
        def _(pe):
            pe.wait_ge(idft_in, 16)
            with pe.Fori(0, PAIRS) as p:
                for k in range(2):
                    pe.wait_ge(yt_in[k], p * 16 + 16)
                    pe.wait_ge(masked, p * 2)
                    for h in range(2):
                        for n in range(NCH):
                            mm = pe.matmul(inv[2 * k + h][:, 0:HALF], yt[:, k, n], idft[:, n, h * HALF:(h + 1) * HALF],
                                           start=(n == 0), stop=(n == NCH - 1))
                    mm.then_inc(inv_ok, 1)

        @block.vector
        def _(dve):
            dve.wait_ge(x_in, 16)
            with dve.Fori(0, PAIRS) as p:
                for k in range(2):
                    dve.wait_ge(inv_ok, p * 2 + k + 1)
                    dve.wait_ge(added, p * 2)
                    for h in range(2):
                        cols = slice(h * HALF, (h + 1) * HALF)
                        v = dve.tensor_tensor(part[:, k, cols], inv[2 * k + h][:, 0:HALF], sp_["mask"][:, cols], ALU.mult)
                    v.then_inc(masked, 1)
                for k in range(2):
                    dve.wait_ge(masked, p * 2 + k + 1)
                    xb = x[:, bass.ds(p * 2 + k, 1), :].rearrange("p a t -> p (a t)")
                    dve.tensor_tensor(xb, xb, part[:, k], ALU.add).then_inc(added, 1)


def layer0_spectral(nc, dram, const, mask):
    with ExitStack() as ctx:
        m = Mem(nc, ctx, "b")
        sp_ = {"mask": mask, "hat": m.sb("hat", [128, FCOLS]), "muw": m.sb("muw", [128, N_LAG, C])}
        with ExitStack() as inner_ctx:
            mi = Mem(nc, inner_ctx, "bu")
            sp_["dft"] = mi.sb("dft", [TT, NT, FCOLS])
            u = mi.sb("u", [128, B, T])
            operator_gates(nc, dram, const, sp_)
            norm_pass(nc, "bn", const, 1,
                      lambda b, h: u[:, bass.ds(b, 1), h * HALF:(h + 1) * HALF].rearrange("p a (h w) -> p (a h) w", w=W),
                      (dram["x1"],))
            spectral_forward(nc, dram, const, sp_, u)
        spectral_apply(nc, dram, const, sp_)


def conv_pass(nc, dram, const, xpad, x):
    with ExitStack() as ctx:
        m = Mem(nc, ctx, "cc")
        w = m.sb("w", [128, TAPS, C])
        bias = m.sb("bias", [128, 1])
        acc = m.banks("acc", 8)
        w_in, conv_ok, added = m.sem("w_in"), m.sem("conv_ok"), m.sem("added")
        block = ctx.enter_context(nc.Block())

        @block.sync
        def _(sp):
            sp.dma_start(w[:], dram["w_conv"]).then_inc(w_in, 16)
            sp.dma_start(bias[:], dram["b_conv"]).then_inc(w_in, 16)

        @block.tensor
        def _(pe):
            pe.wait_ge(w_in, 32)
            with pe.Fori(0, B // 4) as r:
                for k in range(4):
                    pe.wait_ge(added, r * 4)
                    for h in range(2):
                        for tap in range(TAPS):
                            dy, dx = divmod(tap, 3)
                            r0 = h * ROWS + dy
                            mm = pe.matmul(acc[2 * k + h][:, 0:HALF], w[:, tap],
                                           xpad[:, bass.ds(r * 4 + k, 1), r0:r0 + ROWS, dx:dx + W].rearrange("p a h w -> p (a h) w"),
                                           start=(tap == 0), stop=(tap == TAPS - 1))
                    mm.then_inc(conv_ok, 1)

        @block.vector
        def _(dve):
            dve.wait_ge(w_in, 32)
            with dve.Fori(0, B // 4) as r:
                for k in range(4):
                    dve.wait_ge(conv_ok, r * 4 + k + 1)
                    for h in range(2):
                        xb = x[:, bass.ds(r * 4 + k, 1), h * HALF:(h + 1) * HALF].rearrange("p a t -> p (a t)")
                        v = dve.scalar_tensor_tensor(xb, acc[2 * k + h][:, 0:HALF], bias[:, 0:1], xb, ALU.add, ALU.add)
                    v.then_inc(added, 1)


def route_pass(nc, dram, const, z, probs, pooled):
    with ExitStack() as ctx:
        m = Mem(nc, ctx, "cr")
        gw = m.sb("gw", [128, 2 * E])
        gb = m.sb("gb", [128, 1])
        zs = m.sb("zs", [128, 2, T])
        zt = m.sb("zt", [TT, 2, NT, C])
        lg = m.sb("lg", [128, T])
        pr = m.sb("pr", [128, T])
        rest = m.sb("rest", [128, T])
        pt = m.sb("pt", [TT, NT, 2 * E])
        col = m.sb("col", [128, 4])
        top = m.sb("top", [128, TOPK])
        carry = m.sb("carry", [128, 2])
        lgp = m.banks("lgp", 2)
        turned = m.banks("turned", 2)
        pturned = m.banks("pturned", 2)
        pool_p = m.banks("pool", 1)[0]
        w_in, staged, logits_ok, biased, max_ok, neg_ok, exp_ok, inv_ok, pr_ok, top_ok, rest_ok, kept = (
            m.sem(s) for s in ("w_in", "staged", "logits_ok", "biased", "max_ok", "neg_ok", "exp_ok", "inv_ok", "pr_ok",
                               "top_ok", "rest_ok", "kept"))
        turn_ok, zt_ok, pturn_ok, pt_ok, pooled_ok, pooled_taken = (
            m.sem(s) for s in ("turn_ok", "zt_ok", "pturn_ok", "pt_ok", "pooled_ok", "pooled_taken"))
        block = ctx.enter_context(nc.Block())

        @block.sync
        def _(sp):
            sp.dma_start(gw[:], dram["gate_w"]).then_inc(w_in, 16)
            sp.dma_start(gb[:], dram["gate_b"]).then_inc(w_in, 16)

        @block.gpsimd
        def _(pool):
            with pool.Fori(0, PAIRS) as p:
                for k in range(2):
                    pool.wait_ge(turn_ok, p * 2)
                    pool.wait_ge(logits_ok, p * 2)
                    pool.tensor_copy(zs[:, k], z[:, bass.ds(p * 2 + k, 1), :].rearrange("p a t -> p (a t)")).then_inc(staged, 1)

        @block.tensor
        def _(pe):
            pe.wait_ge(w_in, 32)
            with pe.Fori(0, PAIRS) as p:
                pe.wait_ge(staged, p * 2 + 2)
                pe.wait_ge(biased, p)
                for h in range(2):
                    for k in range(2):
                        mm = pe.matmul(lgp[h][E * k:E * (k + 1), 0:HALF], gw[:, 0:E], zs[:, k, h * HALF:(h + 1) * HALF],
                                       start=True, stop=True)
                        mm.then_inc(logits_ok, 1) if h else None
                for k in range(2):
                    pe.wait_ge(zt_ok, p * 2 + k)
                    for i in range(NT):
                        mm = pe.transpose(turned[i // 4][0:TT, (i % 4) * C:(i % 4 + 1) * C],
                                          zs[:, k, i * TT:(i + 1) * TT], const["ident"][:])
                    mm.then_inc(turn_ok, 1)
                pe.wait_ge(kept, p + 1)
                pe.wait_ge(pt_ok, p)
                for i in range(NT):
                    mm = pe.transpose(pturned[i // 4][0:TT, (i % 4) * 128:(i % 4 + 1) * 128], pr[:, i * TT:(i + 1) * TT],
                                      const["ident"][:])
                mm.then_inc(pturn_ok, 1)
                pe.wait_ge(pt_ok, p + 1)
                pe.wait_ge(zt_ok, p * 2 + 2)
                pe.wait_ge(pooled_taken, p)
                for k in range(2):
                    for i in range(NT):
                        mm = pe.matmul(pool_p[:, k * E:(k + 1) * E], zt[:, k, i], pt[:, i, k * E:(k + 1) * E],
                                       start=(i == 0), stop=(i == NT - 1))
                mm.then_inc(pooled_ok, 1)

        @block.scalar
        def _(act):
            act.wait_ge(w_in, 32)
            with act.Fori(0, PAIRS) as p:
                act.wait_ge(logits_ok, p * 2 + 2)
                act.wait_ge(exp_ok, p)
                for h in range(2):
                    a = act.activation(lg[:, h * HALF:(h + 1) * HALF], lgp[h][:, 0:HALF], ACT.Identity, bias=gb[:, 0:1])
                a.then_inc(biased, 1)
                for k in range(2):
                    act.wait_ge(turn_ok, p * 2 + k + 1)
                    act.wait_ge(pooled_ok, p)
                    act.activation(zt[:, k, 0:4].rearrange("p i c -> p (i c)"), turned[0][0:TT, :], ACT.Copy)
                    act.activation(zt[:, k, 4:NT].rearrange("p i c -> p (i c)"), turned[1][0:TT, 0:(NT - 4) * C], ACT.Copy)\
                       .then_inc(zt_ok, 1)
                act.wait_ge(neg_ok, p + 1)
                act.wait_ge(pturn_ok, p)
                act.activation(pr[:], lg[:], ACT.Exp, bias=col[:, 1:2], accum_out=col[:, 2:3]).then_inc(exp_ok, 1)
                act.wait_ge(pturn_ok, p + 1)
                act.activation(pt[:, 0:4].rearrange("p i c -> p (i c)"), pturned[0][0:TT, :], ACT.Copy)
                act.activation(pt[:, 4:NT].rearrange("p i c -> p (i c)"), pturned[1][0:TT, 0:(NT - 4) * 128], ACT.Copy)\
                   .then_inc(pt_ok, 1)

        @block.vector
        def _(dve):
            with dve.Fori(0, PAIRS) as p:
                dve.wait_ge(biased, p + 1)
                dve.tensor_reduce(col[:, 0:1], lg[:], AX_X, ALU.max).then_inc(max_ok, 1)
                dve.wait_ge(max_ok, p + 1)
                dve.tensor_scalar(col[:, 1:2], col[:, 0:1], -1.0, None, ALU.mult).then_inc(neg_ok, 1)
                dve.wait_ge(exp_ok, p + 1)
                dve.reciprocal(col[:, 3:4], col[:, 2:3]).then_inc(inv_ok, 1)
                dve.wait_ge(inv_ok, p + 1)
                dve.tensor_scalar(pr[:], pr[:], col[:, 3:4], None, ALU.mult).then_inc(pr_ok, 1)
                dve.wait_ge(pr_ok, p + 1)
                dve.memset(carry[:, 0:1], 0.0)
                dve.max(top[:], pr[:]).then_inc(top_ok, 1)
                dve.wait_ge(top_ok, p + 1)
                dve.memset(carry[:, 1:2], 0.0)
                dve.match_replace(rest[:], top[:], pr[:], 0.0).then_inc(rest_ok, 1)
                dve.wait_ge(rest_ok, p + 1)
                dve.tensor_tensor(pr[:], pr[:], rest[:], ALU.subtract).then_inc(kept, 1)
                dve.wait_ge(kept, p + 1)
                dve.tensor_copy(probs[:, bass.ds(p, 1), :].rearrange("p a t -> p (a t)"), pr[:])
                dve.wait_ge(pooled_ok, p + 1)
                dve.tensor_copy(pooled[:, :, bass.ds(p * 2, 2)].rearrange("p e k -> p k e"),
                                pool_p[:, 0:2 * E].rearrange("p (k e) -> p k e", k=2)).then_inc(pooled_taken, 1)


def expert_pass(nc, dram, const, pooled, eout):
    NG = E // EG
    with ExitStack() as ctx:
        m = Mem(nc, ctx, "ce")
        w1 = m.sb("w1", [128, 2, EG, HID])
        w2 = m.sb("w2", [128, 2, EG, HC, O])
        b1 = m.sb("b1", [128, E, HC])
        b2 = m.sb("b2", [128, E])
        hid = m.sb("hid", [128, 2, EG, HC, B])
        act_h = m.sb("act_h", [128, 2, EG, HC, B])
        hp = m.banks("hp", 2)
        op = m.banks("op", 2)
        w_in = [m.sem("w_in0"), m.sem("w_in1")]
        b_in, hid_ok, biased, gelu_ok, out_ok, out_taken = (
            m.sem(s) for s in ("b_in", "hid_ok", "biased", "gelu_ok", "out_ok", "out_taken"))
        block = ctx.enter_context(nc.Block())

        @block.sync
        def _(sp):
            sp.dma_start(b1[:], dram["b1"]).then_inc(b_in, 16)
            sp.dma_start(b2[:], dram["b2"]).then_inc(b_in, 16)
            with sp.Fori(0, NG // 2) as r:
                for v in range(2):
                    sp.wait_ge(out_ok, r * 2)
                    sp.dma_start(w1[:, v], dram["w1"][bass.ds((r * 2 + v) * EG, EG)].rearrange("e d h -> d e h")).then_inc(w_in[v], 16)
                    sp.dma_start(w2[:, v], dram["w2"][bass.ds((r * 2 + v) * EG, EG)].rearrange("e p c o -> p e c o")).then_inc(w_in[v], 16)

        @block.tensor
        def _(pe):
            with pe.Fori(0, NG // 2) as r:
                for v in range(2):
                    pe.wait_ge(w_in[v], r * 32 + 32)
                    pe.wait_ge(biased, r * 2)
                    for e in range(EG):
                        for c in range(HC):
                            at = (e * HC + c) * B
                            mm = pe.matmul(hp[v][:, at:at + B], w1[:, v, e, c:HID:HC],
                                           pooled[:, bass.ds((r * 2 + v) * EG + e, 1), :].rearrange("p a b -> p (a b)"),
                                           start=True, stop=True)
                    mm.then_inc(hid_ok, 1)
                for v in range(2):
                    pe.wait_ge(gelu_ok, r * 2 + v + 1)
                    pe.wait_ge(out_taken, r * 2)
                    for e in range(EG):
                        for c in range(HC):
                            mm = pe.matmul(op[v][:, e * B:(e + 1) * B], w2[:, v, e, c], act_h[:, v, e, c],
                                           start=(c == 0), stop=(c == HC - 1))
                    mm.then_inc(out_ok, 1)

        @block.scalar
        def _(act):
            with act.Fori(0, NG // 2) as r:
                for v in range(2):
                    act.wait_ge(biased, r * 2 + v + 1)
                    act.wait_ge(out_ok, r * 2)
                    act.activation(act_h[:, v], hid[:, v], ACT.Gelu).then_inc(gelu_ok, 1)

        @block.vector
        def _(dve):
            dve.wait_ge(b_in, 32)
            with dve.Fori(0, NG // 2) as r:
                for v in range(2):
                    dve.wait_ge(hid_ok, r * 2 + v + 1)
                    dve.wait_ge(gelu_ok, r * 2)
                    dve.tensor_tensor(hid[:, v].rearrange("p e c b -> p (e c) b"),
                                      hp[v][:, 0:EG * HC * B].rearrange("p (e b) -> p e b", b=B),
                                      b1[:, bass.ds((r * 2 + v) * EG, EG), :, None].rearrange("p e c b -> p (e c) b")
                                      .to_broadcast([128, EG * HC, B]), ALU.add).then_inc(biased, 1)
                for v in range(2):
                    dve.wait_ge(out_ok, r * 2 + v + 1)
                    dve.tensor_tensor(eout[:, :, bass.ds((r * 2 + v) * EG, EG)].rearrange("p b e -> p e b"),
                                      op[v][:, 0:EG * B].rearrange("p (e b) -> p e b", b=B),
                                      b2[:, bass.ds((r * 2 + v) * EG, EG), None].to_broadcast([128, EG, B]), ALU.add)\
                       .then_inc(out_taken, 1)


def spread_pass(nc, dram, const, probs, eout, x):
    with ExitStack() as ctx:
        m = Mem(nc, ctx, "cs")
        es = m.sb("es", [128, 2, 2 * E])
        et = m.sb("et", [128, 2, 2, O])
        res = m.sb("res", [128, 2, 2, T])
        turned = m.banks("turned", 2)
        acc = m.banks("acc", 4)
        cleared, staged, turn_ok, et_ok, sum_ok, added = (
            m.sem(s) for s in ("cleared", "staged", "turn_ok", "et_ok", "sum_ok", "added"))
        out = [m.sem("out0"), m.sem("out1")]
        block = ctx.enter_context(nc.Block())

        @block.sync
        def _(sp):
            with sp.Fori(0, PAIRS // 2) as q:
                for v in range(2):
                    sp.wait_ge(added, q * 4 + 2 * v + 2)
                    sp.dma_start(dram["out"][:, bass.ds((q * 2 + v) * 2, 2), :], res[:, v]).then_inc(out[v], 16)
            for v in range(2):
                sp.wait_ge(out[v], 16 * (PAIRS // 2))

        @block.gpsimd
        def _(pool):
            pool.memset(et[:], 0.0).then_inc(cleared, 1)
            with pool.Fori(0, PAIRS // 2) as q:
                for v in range(2):
                    pool.wait_ge(turn_ok, q * 2)
                    pool.tensor_copy(es[:, v], eout[:, bass.ds((q * 2 + v) * 2, 2), :].rearrange("p b e -> p (b e)")).then_inc(staged, 1)

        @block.tensor
        def _(pe):
            with pe.Fori(0, PAIRS // 2) as q:
                for v in range(2):
                    n = q * 2 + v
                    pe.wait_ge(staged, n + 1)
                    pe.wait_ge(et_ok, q * 2)
                    pe.transpose(turned[v][:, 0:O], es[:, v], const["ident"][:]).then_inc(turn_ok, 1)
                for v in range(2):
                    n = q * 2 + v
                    pe.wait_ge(et_ok, n + 1)
                    for k in range(2):
                        pe.wait_ge(added, q * 4 + 2 * v + k - 1 if v or k else q * 4)
                        for h in range(2):
                            mm = pe.matmul(acc[2 * k + h][:, 0:HALF], et[:, v, k],
                                           probs[:, bass.ds(n, 1), h * HALF:(h + 1) * HALF].rearrange("p a t -> p (a t)"),
                                           start=True, stop=True)
                        mm.then_inc(sum_ok, 1)

        @block.scalar
        def _(act):
            act.wait_ge(cleared, 1)
            with act.Fori(0, PAIRS // 2) as q:
                for v in range(2):
                    act.wait_ge(turn_ok, q * 2 + v + 1)
                    act.wait_ge(sum_ok, q * 4)
                    for k in range(2):
                        a = act.activation(et[k * E:(k + 1) * E, v, k], turned[v][k * E:(k + 1) * E, 0:O], ACT.Copy)
                    a.then_inc(et_ok, 1)

        @block.vector
        def _(dve):
            with dve.Fori(0, PAIRS // 2) as q:
                for v in range(2):
                    dve.wait_ge(out[v], q * 16)
                    for k in range(2):
                        dve.wait_ge(sum_ok, q * 4 + 2 * v + k + 1)
                        for h in range(2):
                            cols = slice(h * HALF, (h + 1) * HALF)
                            w = dve.tensor_tensor(res[:, v, k, cols], acc[2 * k + h][:, 0:HALF],
                                                  x[:, bass.ds(q * 4 + 2 * v + k, 1), cols].rearrange("p a t -> p (a t)"), ALU.add)
                        w.then_inc(added, 1)


def zero_images(nc, xpad):
    with ExitStack() as ctx:
        cleared = Mem(nc, ctx, "cz").sem("cleared")
        block = ctx.enter_context(nc.Block())

        @block.gpsimd
        def _(pool):
            pool.memset(xpad[:], 0.0).then_inc(cleared, 1)


def layer1(nc, dram, const, x):
    with ExitStack() as ctx:
        m = Mem(nc, ctx, "cx")
        xpad = m.sb("xpad", [128, B, HP, WP])
        zero_images(nc, xpad)
        norm_pass(nc, "cn", const, 0,
                  lambda b, h: xpad[:, bass.ds(b, 1), 1 + ROWS * h:1 + ROWS * (h + 1), 1:W + 1].rearrange("p a h w -> p (a h) w"), x)
        conv_pass(nc, dram, const, xpad, x)
    with ExitStack() as ctx:
        m = Mem(nc, ctx, "ct")
        probs = m.sb("probs", [128, PAIRS, T])
        pooled = m.sb("pooled", [128, E, B])
        eout = m.sb("eout", [128, B, E])
        with ExitStack() as zctx:
            z = Mem(nc, zctx, "cz").sb("z", [128, B, T])
            norm_pass(nc, "ctn", const, 1,
                      lambda b, h: z[:, bass.ds(b, 1), h * HALF:(h + 1) * HALF].rearrange("p a (h w) -> p (a h) w", w=W), x)
            route_pass(nc, dram, const, z, probs, pooled)
        expert_pass(nc, dram, const, pooled, eout)
        spread_pass(nc, dram, const, probs, eout, x)


def build(nc, dram):
    with ExitStack() as ctx:
        m = Mem(nc, ctx, "k")
        const = {"ident": m.sb("ident", [128, 128]), "mean": m.sb("mean", [128, 128]), "ones": m.sb("ones", [128, HALF]),
                 "eps": m.sb("eps", [128, 2]), "gather": m.sb("gather", [128, 63]), "spread": m.sb("spread", [32, STRIPS, C])}
        mask = m.sb("mask", [128, T])
        phase_constants(nc, dram, const)
        layer0_distance(nc, dram, const)
        layer0_spectral(nc, dram, const, mask)
        x = m.sb("x", [128, B, T])
        spectral_inverse(nc, dram, const, {"mask": mask}, x)
        layer1(nc, dram, const, x)


def _transform_tables(np):
    t = np.arange(T)
    f = np.arange(NF)
    angle = 2.0 * np.pi * np.outer(t, 2 * f + 1) / (2 * 2 * T)
    re, im = np.cos(angle), -np.sin(angle)
    fwd = np.stack([re.reshape(T, NCH, FC), im.reshape(T, NCH, FC)], axis=2)
    fwd = fwd.reshape(NT, TT, FCOLS).transpose(1, 0, 2)
    inv = np.stack([re.T.reshape(NCH, FC, T), im.T.reshape(NCH, FC, T)], axis=1) * (2.0 / (2 * T))
    inv = inv.reshape(NCH, F2, T).transpose(1, 0, 2)
    return np.ascontiguousarray(fwd, np.float32), np.ascontiguousarray(inv, np.float32)


def _layouts(np, x, L0_conv_W, L0_ffn_sigma, L0_ffn_phi, L0_ffn_M_u, L0_ffn_M_phi_plus, L0_ffn_M_phi_minus,
             L0_ffn_log_weights, L0_ffn_gumbel, L1_conv_weights, L1_conv_bias, L1_ffn_gate_w, L1_ffn_gate_b,
             L1_ffn_weight1, L1_ffn_weight2):
    dft, idft = _transform_tables(np)
    mats = np.stack([L0_ffn_M_phi_plus, L0_ffn_M_phi_minus], axis=1)
    w1, w2 = L1_ffn_weight1, L1_ffn_weight2
    arrays = {
        "x": x.reshape(B, C, T).transpose(1, 0, 2),
        "w0": L0_conv_W.reshape(GROUPS, PER_GROUP, C, TAPS).transpose(2, 1, 3, 0),
        "ident": np.eye(128, dtype=np.float32),
        "sigma": np.tile(L0_ffn_sigma, N_OPT * 2).reshape(128, 1),
        "phi": L0_ffn_phi[:T].reshape(NT, TT, K_F).transpose(1, 0, 2),
        "sgn": np.where(np.arange(TT) % 2 == 0, 1.0, -1.0).astype(np.float32).reshape(TT, 1),
        "mu": L0_ffn_M_u.transpose(2, 0, 1, 3),
        "mat": mats.reshape(128, C, C).transpose(0, 2, 1),
        "log_weights": np.broadcast_to(L0_ffn_log_weights, (128, N_OPT)),
        "gumbel": np.broadcast_to(L0_ffn_gumbel, (128, N_OPT)),
        "own": np.repeat(np.eye(N_OPT, dtype=np.float32), 2 * K_F, axis=0),
        "dft": dft,
        "idft": idft,
        "w_conv": L1_conv_weights.reshape(C, C, TAPS).transpose(1, 2, 0),
        "b_conv": L1_conv_bias.reshape(C, 1),
        "gate_w": np.concatenate([L1_ffn_gate_w, L1_ffn_gate_w]).T,
        "gate_b": np.tile(L1_ffn_gate_b, 2).reshape(128, 1),
        "w1": w1[:, :C],
        "b1": w1[:, C].reshape(E, 128, HC).transpose(1, 0, 2),
        "w2": w2[:, :HID].reshape(E, 128, HC, O),
        "b2": w2[:, HID].T,
    }
    return {k: np.ascontiguousarray(v) for k, v in arrays.items()}


SCRATCH = {"base": (C, B, T), "x1": (C, B, T), "x1b": (C, B, T), "uhat": (NCH, C, B, F2), "yt": (NCH, F2, B, C)}


def kernel(**inputs):
    import numpy as np
    import concourse.bacc as bacc
    from concourse.bass_utils import run_bass_kernel_spmd

    nc = bacc.Bacc("TRN2", target_bir_lowering=False, num_devices=1)
    arrays = _layouts(np, **{k: np.asarray(v) for k, v in inputs.items()})
    dram = {k: nc.dram_tensor(f"in_{k}", a.shape, F32, kind="ExternalInput").ap() for k, a in arrays.items()}
    dram |= {k: nc.dram_tensor(f"scratch_{k}", shape, F32).ap() for k, shape in SCRATCH.items()}
    dram["out"] = nc.dram_tensor("out", (C, B, T), F32, kind="ExternalOutput").ap()
    build(nc, dram)
    r = run_bass_kernel_spmd(nc, [{f"in_{k}": a for k, a in arrays.items()}], core_ids=[0])
    out = r.results[0]["out"]
    return np.ascontiguousarray(out.transpose(1, 0, 2)).reshape(B, C, H, W)
```
